# Optimizing a Trainium2 kernel written in Bass

```python
import numpy as np
import jax
import jax.numpy as jnp

def _softmax(x, axis=-1):
    return jax.nn.softmax(x, axis=axis)

def _gelu(x):
    return jax.nn.gelu(x, approximate=True)

def _silu(x):
    return jax.nn.silu(x)

def _sigmoid(x):
    return jax.nn.sigmoid(x)

def _layernorm(x, axis=-1, eps=1e-05):
    m = jnp.mean(x, axis=axis, keepdims=True)
    v = jnp.var(x, axis=axis, keepdims=True)
    return (x - m) / jnp.sqrt(v + eps)

def _scatter_add(tgt, idx, src, axis=0):
    return tgt.at[idx].add(src)

def _segment_sum(src, seg, n):
    return jax.ops.segment_sum(src, seg, n)
kernel_name = 'mk_gnn_resnorm_d1_gnn_r8_782c79'

def setup_inputs(seed: int=0):
    np.random.seed(seed)
    _w = jnp.asarray

    def _rec_inputs():
        import jax
        import jax.numpy as jnp
        _gk = jax.random.key(seed)
        x = -0.000202 + 1 * jax.random.normal(jax.random.fold_in(_gk, 1), (12500, 64), jnp.float32)
        _s = jax.random.randint(jax.random.fold_in(_gk, 2), (200000,), 0, 12500, jnp.int32)
        _d = jax.random.randint(jax.random.fold_in(_gk, 3), (200000,), 0, 12500, jnp.int32)
        _loop = jnp.arange(12500, dtype=jnp.int32)
        src = jnp.concatenate([_s, _d, _loop])
        dst = jnp.concatenate([_d, _s, _loop])
        _o = jnp.argsort(dst, stable=True)
        src = src[_o]
        dst = dst[_o]
        edge_attr_32 = 0.000189758 + 1.00013 * jax.random.normal(jax.random.fold_in(_gk, 11), (412500, 32), jnp.float32)
        return (x, src, dst, edge_attr_32)
    x, src, dst, edge_attr_32 = _rec_inputs()

    def _L0_gnn_setup():
        import jax, jax.numpy as jnp
        import numpy as np
        N, E, D, ED = (12500, 200000, 64, 32)
        LN_EPS = 1e-05
        NEG_SLOPE = 0.2
        key = jax.random.key(seed)
        ks = jax.random.split(key, 12)
        return {'x': jax.random.normal(ks[0], (N, D), jnp.float32), 'edge_index': jax.random.randint(ks[1], (2, E), 0, N, dtype=jnp.int64), 'edge_attr': jax.random.normal(ks[2], (E, ED), jnp.float32), 'We': jax.random.normal(ks[3], (ED, D), jnp.float32) / np.sqrt(ED), 'be': jnp.zeros((D,), jnp.float32), 'W1': jax.random.normal(ks[4], (D, D), jnp.float32) / np.sqrt(D), 'b1': jnp.zeros((D,), jnp.float32), 'W2': jax.random.normal(ks[5], (D, D), jnp.float32) / np.sqrt(D), 'b2': jnp.zeros((D,), jnp.float32), 'eps_gin': jnp.zeros((), jnp.float32), 'gamma': jnp.ones((D,), jnp.float32), 'beta': jnp.zeros((D,), jnp.float32)}
    _L0_gnn_all = _L0_gnn_setup()
    _L0_gnn_in = {k: v for k, v in _L0_gnn_all.items() if k in ('We', 'be', 'W1', 'b1', 'W2', 'b2', 'eps_gin', 'gamma', 'beta')}
    del _L0_gnn_all
    return {'x': x, 'src': src, 'dst': dst, 'edge_attr_32': edge_attr_32, 'L0_gnn_We': _L0_gnn_in['We'], 'L0_gnn_be': _L0_gnn_in['be'], 'L0_gnn_W1': _L0_gnn_in['W1'], 'L0_gnn_b1': _L0_gnn_in['b1'], 'L0_gnn_W2': _L0_gnn_in['W2'], 'L0_gnn_b2': _L0_gnn_in['b2'], 'L0_gnn_eps_gin': _L0_gnn_in['eps_gin'], 'L0_gnn_gamma': _L0_gnn_in['gamma'], 'L0_gnn_beta': _L0_gnn_in['beta']}

def reference(x, src, dst, edge_attr_32, L0_gnn_We, L0_gnn_be, L0_gnn_W1, L0_gnn_b1, L0_gnn_W2, L0_gnn_b2, L0_gnn_eps_gin, L0_gnn_gamma, L0_gnn_beta):
    import jax
    import jax.numpy as jnp

    def _L0_gnn_ref(x, edge_index, edge_attr, We, be, W1, b1, W2, b2, eps_gin, gamma, beta):
        import jax, jax.numpy as jnp
        import numpy as np
        N, E, D, ED = (12500, 200000, 64, 32)
        LN_EPS = 1e-05
        NEG_SLOPE = 0.2
        src, dst = (edge_index[0], edge_index[1])
        msg = jax.nn.relu(x[src] + edge_attr @ We + be)
        aggr = jax.ops.segment_sum(msg, dst, num_segments=x.shape[0])
        h = (1.0 + eps_gin) * x + aggr
        h = jax.nn.relu(h @ W1 + b1) @ W2 + b2
        h = jnp.where(h >= 0, h, NEG_SLOPE * h)
        mu = jnp.mean(h, axis=-1, keepdims=True)
        var = jnp.mean((h - mu) ** 2, axis=-1, keepdims=True)
        return (h - mu) / jnp.sqrt(var + LN_EPS) * gamma + beta
    edge_index = jnp.stack([src, dst])
    x = _layernorm(x + _L0_gnn_ref(x, edge_index, edge_attr_32, L0_gnn_We, L0_gnn_be, L0_gnn_W1, L0_gnn_b1, L0_gnn_W2, L0_gnn_b2, L0_gnn_eps_gin, L0_gnn_gamma, L0_gnn_beta), axis=-1)
    return x

_drawn_inputs = setup_inputs


def setup_inputs(seed=0):
    import zlib

    import numpy as np

    out = dict(_drawn_inputs(seed))
    spreads = {'L0_gnn_be': (0.0, 0.1),
     'L0_gnn_b1': (0.0, 2.0),
     'L0_gnn_b2': (0.0, 0.8),
     'L0_gnn_gamma': (1.0, 0.2),
     'L0_gnn_beta': (0.0, 0.1)}
    factors = {}
    for name, (base, spread) in spreads.items():
        noise = np.random.default_rng([zlib.crc32(name.encode()), seed]).standard_normal(out[name].shape)
        drawn = base * np.exp(spread * noise) if base else spread * noise
        out[name] = jnp.asarray(drawn.astype(out[name].dtype))
    for name, factor in factors.items():
        out[name] = (out[name] * factor).astype(out[name].dtype)
    return out
```

```python
from contextlib import ExitStack

import numpy as np

import concourse.bass as bass
from concourse import mybir

F32 = mybir.dt.float32
BF16 = mybir.dt.bfloat16
I32 = mybir.dt.int32
U32 = mybir.dt.uint32
ALU = mybir.AluOpType
ACT = mybir.ActivationFunctionType
AX_X = mybir.AxisListType.X

P = 128
N, D = 12500, 64
E, ED = 412500, 32
LN_EPS = 1e-05
NEG_SLOPE = 0.2

TG = 8
GE = TG * P
NTILES = -(-E // P)
NG = -(-E // GE)
TAIL_TILES = NTILES - (NG - 1) * TG
SLOTS = 3
ROUNDS = (NG - 1) // SLOTS
assert NG - 1 == ROUNDS * SLOTS
QUARTERS = P // ED
HALVES = TG // QUARTERS

FAR_FROM = 10
FAR_SLOT = SLOTS - 1
NFAR = ROUNDS - FAR_FROM
CB = 8
CLASS = CB * P
NCLASSES = -(-N // CLASS)
CX = CB * D
PIECES = 8
PIECE = NCLASSES * CX // PIECES
assert P * CB == CLASS and CLASS & (CLASS - 1) == 0 and PIECE * PIECES == NCLASSES * CX
assert PIECES <= FAR_FROM

WIN = 64
GWIN = 448

BLOCKS = 7
CN = BLOCKS * P
NCHUNKS = -(-N // CN)
NPAD = NCHUNKS * CN
CW = BLOCKS * D
HALF = CN // 2
ROUNDS_PER_CHUNK = 10
GROUPS_PER_CHUNK = ROUNDS_PER_CHUNK * SLOTS
LEFT_ROUNDS = ROUNDS - (NCHUNKS - 1) * ROUNDS_PER_CHUNK
NW = NPAD // GWIN
assert LEFT_ROUNDS >= 1 and SLOTS == 3 and NPAD % GWIN == 0 and CN % 2 == 0
PARAMS = 7
INNER_STEPS = 8
DVE_STEPS = 16
CENTRED = (5, 14)


def build(nc, x, xT, x_chunks, x_classes, src, dst, far_rows, far_cols, edges, consts, We, be, W1, b1, W2, b2, eps, gamma, beta, out):
    with ExitStack() as ctx:
        def sb(name, shape, dt=F32):
            return ctx.enter_context(nc.sbuf_tensor(name, shape, dt))

        def psum(name, shape):
            return ctx.enter_context(nc.psum_tensor(name, shape, F32))

        def sem(name):
            return ctx.enter_context(nc.semaphore(name))

        hT = sb("hT", [D, NPAD + WIN])
        dst_int = sb("dst_int", [P, NG, TG], I32)
        first_int = sb("first_int", [1, NG], I32)
        first_dst = sb("first_dst", [1, NG])
        rel = sb("rel", [P, NG, TG], I32)
        marks = sb("marks", [P, NG, TG])
        index = sb("index", [P, SLOTS, TG], I32)
        rows = sb("rows", [P, SLOTS, TG * D])
        edge = sb("edge", [P, SLOTS, HALVES * P])
        msg = sb("msg", [P, SLOTS, TG * D])
        onehot = sb("onehot", [P, SLOTS, TG, WIN])
        wide_hot = sb("wide_hot", [P, TG, GWIN])
        rel_g = sb("rel_g", [P, TG])

        x_parts = sb("x_parts", [P, 3, NCLASSES * CX], BF16)
        x_rest = sb("x_rest", [P, PIECE])
        far_src = sb("far_src", [P, P], I32)
        far_key = sb("far_key", [P, P], I32)
        far_hot = sb("far_hot", [P, NCLASSES, P], BF16)
        far_col = sb("far_col", [P, NFAR], I32)
        far_block = sb("far_block", [P, NFAR], I32)
        far_mask = sb("far_mask", [P, NFAR, CB])
        far_picked = sb("far_picked", [P, D, CB])

        const = sb("const", [P, P + GWIN + NG + NCLASSES])
        ident = const[:, 0:P]
        numbers = const[:, P:P + GWIN]
        limits = const[:, P + GWIN:P + GWIN + NG]
        class_node = const[:, P + GWIN + NG:]
        We_diag = sb("We_diag", [P, QUARTERS * D])
        be_all = sb("be_all", [P, D])
        be_rest = sb("be_rest", [P, 2, D])
        be_part = sb("be_part", [P, 3, D], BF16)
        be_rows = sb("be_rows", [P, 3, D], BF16)
        be_group = sb("be_group", [P, TG, D], BF16)
        ones_b = sb("ones_b", [P, P], BF16)
        ones = sb("ones", [P, P])
        W1_wide = sb("W1_wide", [D, P])
        W2_b2 = sb("W2_b2", [D + 1, D])
        b1_col = sb("b1_col", [D, 1])
        eps_col = sb("eps_col", [D, 1])
        eps1 = sb("eps1", [D, 1])
        gamma_sb = sb("gamma_sb", [P, D])
        beta_sb = sb("beta_sb", [P, D])
        ln_eps = sb("ln_eps", [P, 1])
        past = sb("past", [P, NG])
        counts = sb("counts", [P, 2])
        total = sb("total", [1, 1])
        flag = sb("flag", [1, 1], I32)

        a1T = sb("a1T", [D + 1, CN])
        xc = sb("xc", [P, CW])
        y = sb("y", [P, CW])
        sq = sb("sq", [P, CW])
        row_sum = sb("row_sum", [P, 2, BLOCKS])
        neg_mean = sb("neg_mean", [P, 2, BLOCKS])
        sq_sum = sb("sq_sum", [P, 2, BLOCKS])
        std = sb("std", [P, 2, BLOCKS])
        rstd = sb("rstd", [P, 2, BLOCKS])

        pre = psum("pre", [P, SLOTS, 512])
        win = psum("win", [P, 512])
        far_x = psum("far_x", [P, 512])
        dve_const = psum("dve_const", [P, WIN + NCLASSES])
        win_numbers, class_nodes = dve_const[:, 0:WIN], dve_const[:, WIN:]
        ps_half = psum("ps_half", [P, 512])
        ps_node = psum("ps_node", [P, 512])

        dst_loaded, params_loaded, diag_loaded = sem("dst_loaded"), sem("params_loaded"), sem("diag_loaded")
        far_loaded, far_col_loaded, piece_loaded = sem("far_loaded"), sem("far_col_loaded"), sem("piece_loaded")
        first_loaded = sem("first_loaded")
        hT_loaded, const_loaded = sem("hT_loaded"), sem("const_loaded")
        index_loaded = [sem(f"index_loaded{s}") for s in range(SLOTS)]
        edge_loaded = [sem(f"edge_loaded{s}") for s in range(SLOTS)]
        gathered = [sem(f"gathered{s}") for s in range(SLOTS)]
        x_loaded, stored = sem("x_loaded"), sem("stored")
        const_made, diag_zero, setup_step = sem("const_made"), sem("diag_zero"), sem("setup_step")
        first_made, base_spread = sem("first_made"), sem("base_spread")
        counted, totalled, flag_made = sem("counted"), sem("totalled"), sem("flag_made")
        be_made = sem("be_made")
        eps1_made, hT_begun = sem("eps1_made"), sem("hT_begun")
        pre_ready, relu_done, win_ready, added = (
            sem("pre_ready"), sem("relu_done"), sem("win_ready"), sem("added"))
        onehot_ready = sem("onehot_ready")
        wide_made, wide_summed, wide_added, wide_rel = (
            sem("wide_made"), sem("wide_summed"), sem("wide_added"), sem("wide_rel"))
        rows_begun = sem("rows_begun")
        part_copied, part_taken = sem("part_copied"), sem("part_taken")
        far_keyed, far_hot_ready, far_summed = sem("far_keyed"), sem("far_hot_ready"), sem("far_summed")
        far_mask_step, far_picked_step, far_row_ready = (
            sem("far_mask_step"), sem("far_picked_step"), sem("far_row_ready"))
        h1_ready, a1_ready, h2_ready = sem("h1_ready"), sem("a1_ready"), sem("h2_ready")
        y_step, squared, rooted, finished = sem("y_step"), sem("squared"), sem("rooted"), sem("finished")
        y_free = sem("y_free")

        def blocks(ap):
            return ap.rearrange("p (b f) -> p b f", f=D)


        def gather_group(pool, s, nth, tiles=TG):
            pool.wait_ge(index_loaded[s], 16 * nth)
            pool.sem_inc(rows_begun, 1)
            for t in range(tiles):
                pool.indirect_dma_start(
                    out=rows[:, s, t * D:(t + 1) * D], out_offset=None, in_=x,
                    in_offset=bass.IndirectOffsetOnAxis(ap=index[:, s, t:t + 1], axis=0),
                ).then_inc(gathered[s], 16)

        def load_group(sp, g, s):
            sp.dma_start(index[:, s, :], src[g]).then_inc(index_loaded[s], 16)
            sp.dma_start(edge[:, s, :], edges[g]).then_inc(edge_loaded[s], 16)

        def gathers(s, r, far):
            if far and s == FAR_SLOT:
                return 16 * (TG - 1) * (r + 1) + 16 * FAR_FROM
            return 16 * TG * (r + 1)


        def pe_sums(pe, r, s, far=False, last=False):
            pe.wait_ge(relu_done, SLOTS * r + s + 1)
            nc.tensor.matmul(pre[:, s, :], ones_b[:], be_group[:], start=True, stop=False)
            pe.wait_ge(edge_loaded[s], 16 * (r + 1))
            for h in range(HALVES):
                w = QUARTERS * D
                nc.tensor.matmul(pre[:, s, h * w:(h + 1) * w], edge[:, s, h * P:(h + 1) * P], We_diag[:],
                                 start=False, stop=False)
            pe.wait_ge(gathered[s], gathers(s, r, far) - (16 * (TG - TAIL_TILES) if last else 0))
            if far and s == FAR_SLOT:
                pe.wait_ge(far_row_ready, r - FAR_FROM + 1)
            nc.tensor.matmul(pre[:, s, :], ident, rows[:, s, :], start=False, stop=True).then_inc(pre_ready, 1)

        def pe_window(pe, g, s):
            pe.wait_ge(added, g + SLOTS)
            pe.wait_ge(relu_done, g + 1 + SLOTS)
            pe.wait_ge(onehot_ready, g + 1)
            for t in range(TG):
                mm = nc.tensor.matmul(win[0:D, 0:WIN], msg[:, s, t * D:(t + 1) * D], onehot[:, s, t, :],
                                      start=(t == 0), stop=(t == TG - 1))
            mm.then_inc(win_ready, 1)

        def act_messages(act, g, s):
            act.wait_ge(win_ready, g + 1)
            act.wait_ge(pre_ready, g + 1 + SLOTS)
            nc.scalar.activation(msg[:, s, :], pre[:, s, :], ACT.Relu).then_inc(relu_done, 1)

        def dve_onehot(dve, g, s):
            dve.wait_ge(win_ready, g + 1)
            nc.vector.tensor_tensor(
                onehot[:, s, :, :],
                win_numbers.unsqueeze(1).to_broadcast((P, TG, WIN)),
                rel[:, bass.ds(g, 1), :].rearrange("p a t -> p (a t)").unsqueeze(2).to_broadcast((P, TG, WIN)),
                ALU.is_equal).then_inc(onehot_ready, 1)

        def dve_add(dve, g, s):
            first = dve.value_load(dst_int[0:1, bass.ds(g, 1), 0:1], min_val=0, max_val=N - 1)
            to = hT[:, bass.ds(first, WIN)]
            dve.wait_ge(win_ready, g + 1 + SLOTS)
            dve.wait_ge(added, g + SLOTS)
            nc.vector.tensor_tensor(to, win[0:D, 0:WIN], to, ALU.add).then_inc(added, 1)


        def pe_hidden(pe, c, groups_nodeefore):
            pe.wait_ge(added, groups_nodeefore + SLOTS)
            pe.wait_ge(y_step, DVE_STEPS * c + 1)
            for h, ps in enumerate((ps_half, ps_node)):
                nc.tensor.matmul(ps[:, 0:HALF], W1_wide[:], hT[:, bass.ds(c * CN + h * HALF, HALF)],
                                 start=True, stop=True).then_inc(h1_ready, 1)

        def pe_output(pe, c):
            pe.wait_ge(a1_ready, 2 * c + 2)
            for b in range(BLOCKS):
                mm = nc.tensor.matmul(ps_node[:, b * D:(b + 1) * D], a1T[:, b * P:(b + 1) * P], W2_b2[:],
                                      start=True, stop=True)
            mm.then_inc(h2_ready, 1)

        def act_load_x(act, c):
            act.wait_ge(finished, c + 1)
            act.dma_start(xc[:], x_chunks[bass.ds(c, 1)].rearrange("a p f -> (a p) f")).then_inc(x_loaded, 16)

        def act_hidden(act, c):
            for h, ps in enumerate((ps_half, ps_node)):
                act.wait_ge(h1_ready, 2 * c + 1 + h)
                nc.scalar.activation(a1T[0:D, h * HALF:(h + 1) * HALF], ps[0:D, 0:HALF], ACT.Relu,
                                     bias=b1_col[:, 0:1]).then_inc(a1_ready, 1)

        def act_norm(act, c, norm):
            centred = DVE_STEPS * c + CENTRED[norm] + 1
            act.wait_ge(y_step, centred)
            nc.scalar.activation(sq[:], y[:], ACT.Square).then_inc(squared, 1)
            act.wait_ge(y_step, centred + 1)
            nc.scalar.activation(std[:, norm, :], sq_sum[:, norm, :], ACT.Sqrt, bias=ln_eps[:, 0:1],
                                 scale=1.0 / D).then_inc(rooted, 1)

        def act_store(act, c):
            act.wait_ge(finished, c + 2)
            act.dma_start(out[bass.ds(c, 1)].rearrange("a p f -> (a p) f"), y[:]).then_inc(stored, 16)

        def act_stored(act, c):
            act.wait_ge(stored, 16 * (c + 1))
            act.sem_inc(y_free, 1)

        def dve_stepper(dve, c, steps):
            def step(ins):
                steps[0] += 1
                ins.then_inc(y_step, 1)
                dve.wait_ge(y_step, DVE_STEPS * c + 1 + steps[0])
            return step

        def per_block(ap):
            return ap.unsqueeze(2).to_broadcast((P, BLOCKS, D))

        def per_feature(ap):
            return ap.unsqueeze(1).to_broadcast((P, BLOCKS, D))

        def dve_norm(dve, c, norm, step, steps):
            step(nc.vector.tensor_reduce(row_sum[:, norm, :], blocks(y[:]), AX_X, ALU.add))
            step(nc.vector.tensor_scalar(neg_mean[:, norm, :], row_sum[:, norm, :], -1.0 / D, None, ALU.mult))
            step(nc.vector.tensor_tensor(blocks(y[:]), blocks(y[:]), per_block(neg_mean[:, norm, :]), ALU.add))
            assert steps[0] == CENTRED[norm]
            dve.wait_ge(squared, 2 * c + norm + 1)
            step(nc.vector.tensor_reduce(sq_sum[:, norm, :], blocks(sq[:]), AX_X, ALU.add))
            dve.wait_ge(rooted, 2 * c + norm + 1)
            step(nc.vector.reciprocal(rstd[:, norm, :], std[:, norm, :]))
            return nc.vector.tensor_tensor(blocks(y[:]), blocks(y[:]), per_block(rstd[:, norm, :]), ALU.mult)

        def dve_inner(dve, c):
            steps = [0]
            step = dve_stepper(dve, c, steps)
            dve.wait_ge(y_free, c + 1)
            dve.wait_ge(h2_ready, c + 1)
            step(nc.vector.tensor_scalar(y[:], ps_node[:, 0:CW], NEG_SLOPE, None, ALU.mult))
            step(nc.vector.tensor_tensor(y[:], ps_node[:, 0:CW], y[:], ALU.max))
            step(dve_norm(dve, c, 0, step, steps))
            assert steps[0] == INNER_STEPS

        def dve_outer(dve, c):
            steps = [INNER_STEPS]
            step = dve_stepper(dve, c, steps)
            step(nc.vector.tensor_tensor(blocks(y[:]), blocks(y[:]), per_feature(gamma_sb[:]), ALU.mult))
            step(nc.vector.tensor_tensor(blocks(y[:]), blocks(y[:]), per_feature(beta_sb[:]), ALU.add))
            dve.wait_ge(x_loaded, 16 * (c + 1))
            step(nc.vector.tensor_tensor(y[:], y[:], xc[:], ALU.add))
            dve_norm(dve, c, 1, step, steps).then_inc(finished, 1)
            assert steps[0] == DVE_STEPS


        def act_load_piece(act, r):
            act.wait_ge(part_copied, 3 * r + 1)
            act.dma_start(x_rest[:], x_classes[bass.ds(r, 1)].rearrange("a p f -> (a p) f")).then_inc(piece_loaded, 16)

        def act_copy_parts(act, r):
            act.wait_ge(piece_loaded, 16 * (r + 1))
            for part in range(3):
                if part:
                    act.wait_ge(part_taken, 2 * r + part + 1)
                nc.scalar.activation(x_parts[:, part, bass.ds(r * PIECE, PIECE)], x_rest[:], ACT.Copy).then_inc(part_copied, 1)

        def dve_take_parts(dve, r):
            for part in range(2):
                dve.wait_ge(part_copied, 3 * r + part + 2)
                nc.vector.tensor_tensor(x_rest[:], x_rest[:], x_parts[:, part, bass.ds(r * PIECE, PIECE)],
                                        ALU.subtract).then_inc(part_taken, 1)

        def dve_far_masks(dve):
            dve.wait_ge(far_col_loaded, 16)
            nc.vector.tensor_scalar(far_block[:], far_col[:], P.bit_length() - 1, CB - 1, ALU.logical_shift_right,
                                    ALU.bitwise_and).then_inc(far_mask_step, 1)
            dve.wait_ge(far_mask_step, 1)
            nc.vector.tensor_tensor(far_mask[:], far_block[:].unsqueeze(2).to_broadcast((P, NFAR, CB)),
                                    win_numbers[:, 0:CB].unsqueeze(1).to_broadcast((P, NFAR, CB)),
                                    ALU.is_equal).then_inc(far_mask_step, 1)
            dve.wait_ge(far_mask_step, 2)

        def dve_far_hot(dve, r):
            i = r - FAR_FROM
            dve.wait_ge(far_loaded, 16 * (i + 1))
            nc.vector.tensor_scalar(far_key[:], far_src[:], ~((CB - 1) * P), None, ALU.bitwise_and).then_inc(far_keyed, 1)
            dve.wait_ge(far_keyed, i + 2)
            dve.wait_ge(far_summed, i + 1)
            nc.vector.tensor_tensor(far_hot[:], far_key[:].unsqueeze(1).to_broadcast((P, NCLASSES, P)),
                                    class_nodes.unsqueeze(2).to_broadcast((P, NCLASSES, P)),
                                    ALU.is_equal).then_inc(far_hot_ready, 1)

        def pe_far(pe, r):
            i = r - FAR_FROM
            pe.wait_ge(far_hot_ready, i + 2)
            pe.wait_ge(far_picked_step, 2 * i + 1)
            for k in range(NCLASSES):
                for part in range(3):
                    mm = nc.tensor.matmul(far_x[:], far_hot[:, k, :], x_parts[:, part, k * CX:(k + 1) * CX],
                                          start=(k == 0 and part == 0), stop=(k == NCLASSES - 1 and part == 2))
            mm.then_inc(far_summed, 1)

        def dve_far_pick(dve, r):
            i = r - FAR_FROM
            dve.wait_ge(far_summed, i + 2)
            dve.wait_ge(far_picked_step, 2 * i + 1)
            nc.vector.tensor_tensor(
                far_picked[:], far_x[:].rearrange("p (f b) -> p f b", b=CB),
                far_mask[:, bass.ds(i, 1), :].to_broadcast((P, D, CB)), ALU.mult).then_inc(far_picked_step, 1)
            dve.wait_ge(far_picked_step, 2 * i + 2)
            dve.wait_ge(pre_ready, SLOTS * r + FAR_SLOT + 1)
            reduced = nc.vector.tensor_reduce(rows[:, FAR_SLOT, (TG - 1) * D:], far_picked[:], AX_X, ALU.add)
            reduced.then_inc(far_row_ready, 1)
            dve.wait_ge(far_row_ready, i + 1)
            dve.sem_inc(far_picked_step, 1)


        def sp_round(sp, r, far, slots=SLOTS):
            for s in range(slots):
                g = SLOTS * r + s
                sp.wait_ge(gathered[s], gathers(s, r - 1, far))
                sp.dma_start(index[:, s, :], src[bass.ds(g, 1)].rearrange("a p t -> (a p) t")).then_inc(index_loaded[s], 16)
                sp.wait_ge(pre_ready, g + 1)
                sp.dma_start(edge[:, s, :], edges[bass.ds(g, 1)].rearrange("a p e -> (a p) e")).then_inc(edge_loaded[s], 16)

        def sp_far_round(sp, r):
            sp.wait_ge(far_hot_ready, r - FAR_FROM + 1)
            sp.dma_start(far_src[:], far_rows[bass.ds(r - FAR_FROM, 1), :].to_broadcast((P, P))).then_inc(far_loaded, 16)
            sp_round(sp, r, far=True)

        def pool_round(pool, r, far, slots=SLOTS):
            for s in range(slots):
                pool.wait_ge(pre_ready, SLOTS * r + s + 1)
                gather_group(pool, s, r + 1, TG - 1 if far and s == FAR_SLOT else TG)

        def pool_tail(pool):
            pool.wait_ge(pre_ready, NG)
            gather_group(pool, 0, ROUNDS + 1, TAIL_TILES)

        def windowed(eng):
            eng.wait_ge(flag_made, 1)
            return eng.value_load(flag[0:1, 0:1], min_val=0, max_val=1) == 1

        with nc.Block() as block:
            @block.sync
            def _(sp):
                with nc.allow_non_contiguous_dma(reason="one dst of each group"):
                    sp.dma_start(first_int[:], dst[0:1, :, 0]).then_inc(first_loaded, 16)
                for s in range(SLOTS):
                    sp.dma_start(index[:, s, :], src[s]).then_inc(index_loaded[s], 16)
                sp.dma_start(dst_int[:], dst).then_inc(dst_loaded, 16)
                sp.dma_start(const[:], consts).then_inc(const_loaded, 16)
                for s in range(SLOTS):
                    sp.dma_start(edge[:, s, :], edges[s]).then_inc(edge_loaded[s], 16)
                sp.wait_ge(diag_zero, 1)
                for q in range(QUARTERS):
                    sp.dma_start(We_diag[q * ED:(q + 1) * ED, q * D:(q + 1) * D], We).then_inc(diag_loaded, 16)
                sp.dma_start(W1_wide[:, 0:D], W1).then_inc(diag_loaded, 16)
                sp.dma_start(far_col[:], far_cols).then_inc(far_col_loaded, 16)

                with sp.If(windowed(sp)):
                    with sp.Fori(1, FAR_FROM) as r:
                        sp_round(sp, r, far=False)
                    with sp.Fori(FAR_FROM, ROUNDS) as r:
                        sp_far_round(sp, r)
                    sp_round(sp, ROUNDS, far=True, slots=1)
                with sp.Else():
                    with sp.Fori(1, ROUNDS) as r:
                        sp_round(sp, r, far=False)
                    sp_round(sp, ROUNDS, far=False, slots=1)

            @block.gpsimd
            def _(pool):
                for s in range(SLOTS):
                    gather_group(pool, s, 1)

                with pool.If(windowed(pool)):
                    with pool.Fori(1, FAR_FROM) as r:
                        pool_round(pool, r, far=False)
                    with pool.Fori(FAR_FROM, ROUNDS) as r:
                        pool_round(pool, r, far=True)
                    pool_tail(pool)
                with pool.Else():
                    with pool.Fori(1, ROUNDS) as r:
                        pool_round(pool, r, far=False)
                    pool_tail(pool)

            @block.scalar
            def _(act):
                params = [(eps_col[:], eps.to_broadcast((D, 1))),
                          (be_all[:], be.to_broadcast((P, D))),
                          (W2_b2[0:D, :], W2), (W2_b2[D:D + 1, :], b2), (b1_col[:], b1),
                          (gamma_sb[:], gamma.to_broadcast((P, D))),
                          (beta_sb[:], beta.to_broadcast((P, D)))]
                assert len(params) == PARAMS
                for to, of in params:
                    act.dma_start(to, of).then_inc(params_loaded, 16)
                act.dma_start(hT[:, 0:NPAD], xT).then_inc(hT_loaded, 16)
                act.wait_ge(eps1_made, 1)
                act.wait_ge(hT_loaded, 16)
                nc.scalar.activation(hT[:, 0:NPAD], hT[:, 0:NPAD], ACT.Copy, scale=eps1[:, 0:1]).then_inc(hT_begun, 1)

                def group(r, s):
                    act_messages(act, r * SLOTS + s, s)

                def rounds(start, end):
                    with act.Fori(start, end) as r:
                        for s in range(SLOTS):
                            group(r, s)

                def finishing_round(c, r):
                    act_hidden(act, c)
                    group(r, 0)
                    act_norm(act, c, 0)
                    group(r, 1)
                    act_norm(act, c, 1)
                    group(r, 2)
                    act_store(act, c)

                with act.If(windowed(act)):
                    act_load_x(act, 0)
                    with act.Fori(0, PIECES) as r:
                        act_load_piece(act, r)
                        for s in range(SLOTS):
                            group(r, s)
                        act_copy_parts(act, r)
                    rounds(PIECES, ROUNDS_PER_CHUNK)
                    with act.Fori(0, NCHUNKS - 2) as c:
                        finishing_round(c, (c + 1) * ROUNDS_PER_CHUNK)
                        with act.Fori(1, ROUNDS_PER_CHUNK) as r:
                            for s in range(SLOTS):
                                group((c + 1) * ROUNDS_PER_CHUNK + r, s)
                        act_stored(act, c)
                        act_load_x(act, c + 1)
                    finishing_round(NCHUNKS - 2, ROUNDS - LEFT_ROUNDS)
                    rounds(ROUNDS - LEFT_ROUNDS + 1, ROUNDS)
                    act_stored(act, NCHUNKS - 2)
                    act_load_x(act, NCHUNKS - 1)
                    group(ROUNDS, 0)
                    act_hidden(act, NCHUNKS - 1)
                    act_norm(act, NCHUNKS - 1, 0)
                    act_norm(act, NCHUNKS - 1, 1)
                    act_store(act, NCHUNKS - 1)
                    act.wait_ge(stored, 16 * NCHUNKS)
                with act.Else():
                    rounds(0, ROUNDS)
                    group(ROUNDS, 0)
                    with act.Fori(0, NCHUNKS) as c:
                        act_load_x(act, c)
                        act_hidden(act, c)
                        act_norm(act, c, 0)
                        act_norm(act, c, 1)
                        act_store(act, c)
                        act_stored(act, c)
                    act.wait_ge(stored, 16 * NCHUNKS)

            @block.tensor
            def _(pe):
                pe.wait_ge(const_made, 1)
                pe.wait_ge(first_made, 1)
                nc.tensor.matmul(ps_node[:, 0:NG], ones[0:1, :], first_dst[:], start=True, stop=True).then_inc(base_spread, 1)
                pe.wait_ge(be_made, 1)
                pe.wait_ge(diag_loaded, 16 * (QUARTERS + 1))
                pe.wait_ge(counted, 1)
                nc.tensor.matmul(ps_half[0:1, 0:2], ones[:, 0:1], counts[:], start=True, stop=True).then_inc(totalled, 1)

                def group(r, s, far=False, last=False):
                    pe_sums(pe, r, s, far, last)
                    pe_window(pe, r * SLOTS + s, s)

                def far_round(r):
                    group(r, 0, far=True)
                    pe_far(pe, r)
                    group(r, 1, far=True)
                    group(r, 2, far=True)

                def finishing_round(c, r):
                    pe_hidden(pe, c, r * SLOTS)
                    group(r, 0, far=True)
                    pe_output(pe, c)
                    pe_far(pe, r)
                    group(r, 1, far=True)
                    group(r, 2, far=True)

                def wide_group(r, s, last=False):
                    g = r * SLOTS + s
                    pe_sums(pe, r, s, False, last)
                    with pe.Fori(0, NW) as w:
                        pe.wait_ge(relu_done, g + 1 + SLOTS)
                        pe.wait_ge(wide_made, g * NW + w + 1)
                        for t in range(TG):
                            mm = nc.tensor.matmul(win[0:D, 0:GWIN], msg[:, s, t * D:(t + 1) * D],
                                                  wide_hot[:, t, :], start=(t == 0), stop=(t == TG - 1))
                        mm.then_inc(wide_summed, 1)
                    pe.wait_ge(wide_added, (g + 1) * NW)
                    pe.sem_inc(win_ready, 1)

                with pe.If(windowed(pe)):
                    with pe.Fori(0, ROUNDS_PER_CHUNK) as r:
                        for s in range(SLOTS):
                            group(r, s)
                    with pe.Fori(0, NCHUNKS - 2) as c:
                        finishing_round(c, (c + 1) * ROUNDS_PER_CHUNK)
                        with pe.Fori(1, ROUNDS_PER_CHUNK) as r:
                            far_round((c + 1) * ROUNDS_PER_CHUNK + r)
                    finishing_round(NCHUNKS - 2, ROUNDS - LEFT_ROUNDS)
                    with pe.Fori(ROUNDS - LEFT_ROUNDS + 1, ROUNDS) as r:
                        far_round(r)
                    group(ROUNDS, 0, far=True, last=True)
                    pe_hidden(pe, NCHUNKS - 1, NG)
                    pe_output(pe, NCHUNKS - 1)
                with pe.Else():
                    with pe.Fori(0, ROUNDS) as r:
                        for s in range(SLOTS):
                            wide_group(r, s)
                    wide_group(ROUNDS, 0, last=True)
                    with pe.Fori(0, NCHUNKS) as c:
                        pe_hidden(pe, c, 0)
                        pe_output(pe, c)

            @block.vector
            def _(dve):
                steps = [0]

                def then(ins):
                    steps[0] += 1
                    ins.then_inc(setup_step, 1)
                    dve.wait_ge(setup_step, steps[0])

                nc.vector.memset(W1_wide[:], 0.0)
                nc.vector.memset(We_diag[:], 0.0).then_inc(diag_zero, 1)
                nc.vector.memset(ones[:], 1.0).then_inc(const_made, 1)
                nc.vector.memset(ones_b[:], 1.0)
                nc.vector.memset(ln_eps[:], LN_EPS)
                nc.vector.memset(hT[:, NPAD:NPAD + WIN], 0.0)
                nc.vector.memset(a1T[D:D + 1, :], 1.0)
                for begins_at_slots in (pre_ready, relu_done, win_ready, added):
                    dve.sem_inc(begins_at_slots, SLOTS)
                for begins_at_one in (y_step, finished, y_free, wide_summed, part_copied, part_taken,
                                      far_keyed, far_hot_ready, far_summed, far_picked_step):
                    dve.sem_inc(begins_at_one, 1)
                dve.wait_ge(first_loaded, 16)
                nc.vector.tensor_copy(first_dst[:], first_int[:]).then_inc(first_made, 1)
                dve.wait_ge(params_loaded, 16 * PARAMS)
                nc.vector.tensor_scalar(eps1[:], eps_col[:], 1.0, None, ALU.add).then_inc(eps1_made, 1)
                dve.wait_ge(base_spread, 1)
                dve.wait_ge(dst_loaded, 16)
                base = ps_node[:, 0:NG]
                then(nc.vector.tensor_tensor(rel[:], dst_int[:], base.unsqueeze(2).to_broadcast((P, NG, TG)),
                                             ALU.subtract))
                then(nc.vector.tensor_scalar(marks[:], rel[:].bitcast(U32), float(WIN), 0.0, ALU.is_lt, ALU.add,
                                             accum_out=counts[:, 0:1]))
                dve.wait_ge(const_loaded, 16)
                then(nc.vector.tensor_tensor(past[:], base, limits, ALU.is_ge))
                nc.vector.tensor_reduce(counts[:, 1:2], past[:], AX_X, ALU.add).then_inc(counted, 1)
                then(nc.vector.tensor_copy(be_part[:, 0, :], be_all[:]))
                then(nc.vector.tensor_tensor(be_rest[:, 0, :], be_all[:], be_part[:, 0, :], ALU.subtract))
                then(nc.vector.tensor_copy(be_part[:, 1, :], be_rest[:, 0, :]))
                then(nc.vector.tensor_tensor(be_rest[:, 1, :], be_rest[:, 0, :], be_part[:, 1, :], ALU.subtract))
                then(nc.vector.tensor_copy(be_part[:, 2, :], be_rest[:, 1, :]))
                then(nc.vector.tensor_scalar(be_rows[:, 0, :], be_part[:, 0, :], ident[:, 0:1], None, ALU.mult))
                for k in (1, 2):
                    then(nc.vector.scalar_tensor_tensor(
                        out=be_rows[:, k, :], in0=be_part[:, k, :], scalar=ident[:, k:k + 1],
                        in1=be_rows[:, k - 1, :], op0=ALU.mult, op1=ALU.add))
                nc.vector.tensor_copy(be_group[:], be_rows[:, 2, :].unsqueeze(1).to_broadcast((P, TG, D))).then_inc(be_made, 1)
                nc.vector.tensor_copy(win_numbers, numbers[:, 0:WIN])
                then(nc.vector.tensor_copy(class_nodes, class_node))
                dve.wait_ge(totalled, 1)
                then(nc.vector.tensor_scalar(total[:], ps_half[0:1, 0:1], float(E), None, ALU.is_equal))
                nc.vector.scalar_tensor_tensor(out=flag[:], in0=ps_half[0:1, 1:2], scalar=float(P * NG), in1=total[:],
                                               op0=ALU.is_equal, op1=ALU.mult).then_inc(flag_made, 1)
                dve.wait_ge(hT_begun, 1)

                def group(r, s):
                    dve_onehot(dve, r * SLOTS + s, s)
                    dve_add(dve, r * SLOTS + s, s)

                def far_round(r):
                    dve_far_hot(dve, r)
                    group(r, 0)
                    dve_far_pick(dve, r)
                    group(r, 1)
                    group(r, 2)

                def finishing_round(c, r):
                    g = r * SLOTS
                    dve_far_hot(dve, r)
                    group(r, 0)
                    dve_onehot(dve, g + 1, 1)
                    dve_inner(dve, c)
                    dve_far_pick(dve, r)
                    dve_add(dve, g + 1, 1)
                    dve_onehot(dve, g + 2, 2)
                    dve_outer(dve, c)
                    dve_add(dve, g + 2, 2)

                with dve.If(windowed(dve)):
                    dve_far_masks(dve)
                    with dve.Fori(0, PIECES) as r:
                        for s in range(SLOTS):
                            group(r, s)
                        dve_take_parts(dve, r)
                    with dve.Fori(PIECES, ROUNDS_PER_CHUNK) as r:
                        for s in range(SLOTS):
                            group(r, s)
                    with dve.Fori(0, NCHUNKS - 2) as c:
                        finishing_round(c, (c + 1) * ROUNDS_PER_CHUNK)
                        with dve.Fori(1, ROUNDS_PER_CHUNK) as r:
                            far_round((c + 1) * ROUNDS_PER_CHUNK + r)
                    finishing_round(NCHUNKS - 2, ROUNDS - LEFT_ROUNDS)
                    with dve.Fori(ROUNDS - LEFT_ROUNDS + 1, ROUNDS) as r:
                        far_round(r)
                    group(ROUNDS, 0)
                    dve_inner(dve, NCHUNKS - 1)
                    dve_outer(dve, NCHUNKS - 1)
                with dve.Else():
                    with dve.Fori(0, NG) as g:
                        nc.vector.tensor_copy(rel_g[:], dst_int[:, bass.ds(g, 1), :].rearrange("p a t -> p (a t)")).then_inc(wide_rel, 1)
                        with dve.Fori(0, NW) as w:
                            dve.wait_ge(wide_rel, g * (NW + 1) + w + 1)
                            dve.wait_ge(wide_summed, g * NW + w + 1)
                            nc.vector.tensor_tensor(
                                wide_hot[:], numbers.unsqueeze(1).to_broadcast((P, TG, GWIN)),
                                rel_g[:].unsqueeze(2).to_broadcast((P, TG, GWIN)), ALU.is_equal).then_inc(wide_made, 1)
                            dve.wait_ge(wide_made, g * NW + w + 1)
                            nc.vector.tensor_scalar(rel_g[:], rel_g[:], -float(GWIN), None, ALU.add).then_inc(wide_rel, 1)
                            dve.wait_ge(wide_summed, g * NW + w + 2)
                            to = hT[:, bass.ds(w * GWIN, GWIN)]
                            nc.vector.tensor_tensor(to, win[0:D, 0:GWIN], to, ALU.add).then_inc(wide_added, 1)
                        dve.wait_ge(wide_rel, (g + 1) * (NW + 1))
                    dve.wait_ge(wide_added, NG * NW)
                    with dve.Fori(0, NCHUNKS) as c:
                        dve_inner(dve, c)
                        dve_outer(dve, c)


def kernel(x, src, dst, edge_attr_32, L0_gnn_We, L0_gnn_be, L0_gnn_W1, L0_gnn_b1, L0_gnn_W2, L0_gnn_b2,
           L0_gnn_eps_gin, L0_gnn_gamma, L0_gnn_beta):
    import concourse.bacc as bacc
    from concourse.bass_utils import run_bass_kernel_spmd

    x, src, dst, edge_attr = (np.asarray(a) for a in (x, src, dst, edge_attr_32))
    epad = NG * GE - E
    x_padded = np.pad(x, ((0, NPAD - N), (0, 0)))
    src_l = np.pad(src, (0, epad)).reshape(NG, TG, P).transpose(0, 2, 1)
    dst_l = np.pad(dst, (0, epad), constant_values=-1).reshape(NG, TG, P).transpose(2, 0, 1)
    edges = np.pad(edge_attr, ((0, epad), (0, 0))).reshape(NG, HALVES, QUARTERS, P, ED)
    edges = edges.transpose(0, 2, 4, 1, 3).reshape(NG, P, HALVES * P)
    x_classes = np.pad(x, ((0, NCLASSES * CLASS - N), (0, 0))).reshape(NCLASSES, CB, P, D)
    x_classes = x_classes.transpose(2, 0, 3, 1).reshape(P, PIECES, PIECE).transpose(1, 0, 2)
    far = src_l[FAR_FROM * SLOTS + FAR_SLOT:NG - 1:SLOTS, :, TG - 1]
    chunk = np.minimum(np.arange(NG) // GROUPS_PER_CHUNK, NCHUNKS - 1)
    consts = np.concatenate([np.eye(P), np.tile(np.arange(GWIN), (P, 1)), np.tile(CN * chunk, (P, 1)),
                             CLASS * np.arange(NCLASSES)[None, :] + np.arange(P)[:, None]], 1)
    given = {
        "x_rows": x,
        "x_T": x_padded.T,
        "x_chunks": x_padded.reshape(NCHUNKS, BLOCKS, P, D).transpose(0, 2, 1, 3).reshape(NCHUNKS, P, CW),
        "x_classes": x_classes,
        "src_groups": src_l,
        "dst_groups": dst_l,
        "far_rows": far,
        "far_cols": far.T,
        "edge_groups": edges,
        "consts": consts.astype(np.float32),
        "We": L0_gnn_We, "be": np.reshape(L0_gnn_be, (1, D)),
        "W1": L0_gnn_W1, "b1": np.reshape(L0_gnn_b1, (D, 1)),
        "W2": L0_gnn_W2, "b2": np.reshape(L0_gnn_b2, (1, D)),
        "eps": np.reshape(L0_gnn_eps_gin, (1, 1)),
        "gamma": np.reshape(L0_gnn_gamma, (1, D)), "beta": np.reshape(L0_gnn_beta, (1, D)),
    }
    nc = bacc.Bacc("TRN2", target_bir_lowering=False, num_devices=1)
    arrays = {name: np.ascontiguousarray(a) for name, a in given.items()}
    args = [nc.dram_tensor(name, a.shape, mybir.dt.from_np(a.dtype), kind="ExternalInput").ap()
            for name, a in arrays.items()]
    out = nc.dram_tensor("out", (NCHUNKS, P, CW), F32, kind="ExternalOutput").ap()
    build(nc, *args, out)
    got = run_bass_kernel_spmd(nc, [arrays], core_ids=[0]).results[0]["out"]
    return got.reshape(NCHUNKS, P, BLOCKS, D).transpose(0, 2, 1, 3).reshape(NPAD, D)[:N]
```

```python
from contextlib import ExitStack

import numpy as np

import concourse.bass as bass
from concourse import mybir

F32 = mybir.dt.float32
BF16 = mybir.dt.bfloat16
I32 = mybir.dt.int32
U32 = mybir.dt.uint32
ALU = mybir.AluOpType
ACT = mybir.ActivationFunctionType
AX_X = mybir.AxisListType.X

P = 128
N, D = 12500, 64
E, ED = 412500, 32
LN_EPS = 1e-05
NEG_SLOPE = 0.2

TG = 8
GE = TG * P
NTILES = -(-E // P)
NG = -(-E // GE)
TAIL_TILES = NTILES - (NG - 1) * TG
SLOTS = 3
TURN = 2 * SLOTS
TURNS = (NG - 1) // TURN
assert NG - 1 == TURNS * TURN
QUARTERS = P // ED
HALVES = TG // QUARTERS

FAR_TURN = 5
NFAR = (TURNS - FAR_TURN) * SLOTS
CB = 8
CLASS = CB * P
NCLASSES = -(-N // CLASS)
CX = CB * D
PIECES = 8
PIECE = NCLASSES * CX // PIECES
assert P * CB == CLASS and CLASS & (CLASS - 1) == 0 and PIECE * PIECES == NCLASSES * CX
assert PIECES == 2 * (FAR_TURN - 1)

WIN = 64
GWIN = 448

BLOCKS = 7
CN = BLOCKS * P
NCHUNKS = -(-N // CN)
NPAD = NCHUNKS * CN
CW = BLOCKS * D
HALF = CN // 2
TURNS_PER_CHUNK = 5
GROUPS_PER_CHUNK = TURNS_PER_CHUNK * TURN
LEFT_TURNS = TURNS - (NCHUNKS - 1) * TURNS_PER_CHUNK
NW = NPAD // GWIN
assert LEFT_TURNS >= 1 and SLOTS == 3 and FAR_TURN == TURNS_PER_CHUNK and NPAD % GWIN == 0 and CN % 2 == 0
PARAMS = 7
INNER_STEPS = 7
DVE_STEPS = 14
CENTRED = (4, 12)


def build(nc, x, xT, x_chunks, x_classes, src, dst, far_rows, far_cols, edges, consts, We, be, W1, b1, W2, b2,
          eps, gamma, beta, out):
    with ExitStack() as ctx:
        def sb(name, shape, dt=F32):
            return ctx.enter_context(nc.sbuf_tensor(name, shape, dt))

        def psum(name, shape):
            return ctx.enter_context(nc.psum_tensor(name, shape, F32))

        def sem(name):
            return ctx.enter_context(nc.semaphore(name))

        hT = sb("hT", [D, NPAD + WIN])
        dst_int = sb("dst_int", [P, NG, TG], I32)
        first_int = sb("first_int", [1, NG], I32)
        first_dst = sb("first_dst", [1, NG])
        rel = sb("rel", [P, NG, TG], I32)
        marks = sb("marks", [P, NG, TG])
        index = sb("index", [P, SLOTS, TG], I32)
        rows = sb("rows", [P, SLOTS, TG * D])
        edge = sb("edge", [P, SLOTS, HALVES * P])
        msg = sb("msg", [P, SLOTS, TG * D])
        onehot = sb("onehot", [P, SLOTS, TG, WIN])
        wide_hot = sb("wide_hot", [P, TG, GWIN])
        rel_g = sb("rel_g", [P, TG])

        x_parts = sb("x_parts", [P, 3, NCLASSES * CX], BF16)
        x_rest = sb("x_rest", [P, PIECE])
        far_src = sb("far_src", [P, P], I32)
        far_key = sb("far_key", [P, P], I32)
        far_hot = sb("far_hot", [P, NCLASSES, P], BF16)
        far_col = sb("far_col", [P, NFAR], I32)
        far_block = sb("far_block", [P, NFAR], I32)
        far_mask = sb("far_mask", [P, NFAR, CB])
        far_picked = sb("far_picked", [P, D, CB])

        const = sb("const", [P, 3 + GWIN + NG + NCLASSES])
        unit = const[:, 0:3]
        numbers = const[:, 3:3 + GWIN]
        limits = const[:, 3 + GWIN:3 + GWIN + NG]
        class_node = const[:, 3 + GWIN + NG:]
        We_diag = sb("We_diag", [P, QUARTERS * D])
        be_all = sb("be_all", [P, D])
        be_rest = sb("be_rest", [P, 2, D])
        be_part = sb("be_part", [P, 3, D], BF16)
        be_rows = sb("be_rows", [P, 3, D], BF16)
        be_group = sb("be_group", [P, TG, D], BF16)
        ones_b = sb("ones_b", [P, P], BF16)
        ones = sb("ones", [P, P])
        W1_wide = sb("W1_wide", [D, P])
        W2_b2 = sb("W2_b2", [D + 1, D])
        b1_col = sb("b1_col", [D, 1])
        eps_col = sb("eps_col", [D, 1])
        eps1 = sb("eps1", [D, 1])
        gamma_sb = sb("gamma_sb", [P, D])
        beta_sb = sb("beta_sb", [P, D])
        ln_eps = sb("ln_eps", [P, 1])
        past = sb("past", [P, NG])
        counts = sb("counts", [P, 2])
        total = sb("total", [1, 1])
        flag = sb("flag", [1, 1], I32)

        a1T = sb("a1T", [D + 1, CN])
        xc = sb("xc", [P, CW])
        y = sb("y", [P, CW])
        sq = sb("sq", [P, CW])
        row_sum = sb("row_sum", [P, 2, BLOCKS])
        sq_sum = sb("sq_sum", [P, 2, BLOCKS])
        std = sb("std", [P, 2, BLOCKS])
        rstd = sb("rstd", [P, 2, BLOCKS])

        pre = psum("pre", [P, SLOTS, 512])
        win = psum("win", [P, 512])
        far_x = psum("far_x", [P, 512])
        dve_const = psum("dve_const", [P, WIN + NCLASSES])
        win_numbers, class_nodes = dve_const[:, 0:WIN], dve_const[:, WIN:]
        ps_half = psum("ps_half", [P, 512])
        ps_node = psum("ps_node", [P, 512])

        dst_loaded, params_loaded, diag_loaded = sem("dst_loaded"), sem("params_loaded"), sem("diag_loaded")
        far_loaded, far_col_loaded, piece_loaded = sem("far_loaded"), sem("far_col_loaded"), sem("piece_loaded")
        first_loaded = sem("first_loaded")
        hT_loaded, const_loaded = [sem("hT_loaded0"), sem("hT_loaded1")], sem("const_loaded")
        index_loaded = [sem(f"index_loaded{s}") for s in range(SLOTS)]
        edge_loaded = [sem(f"edge_loaded{s}") for s in range(SLOTS)]
        gathered = [sem(f"gathered{s}") for s in range(SLOTS)]
        x_loaded, stored = sem("x_loaded"), sem("stored")
        const_made, diag_zero, setup_step = sem("const_made"), sem("diag_zero"), sem("setup_step")
        first_made, base_spread = sem("first_made"), sem("base_spread")
        counted, totalled, flag_made = sem("counted"), sem("totalled"), sem("flag_made")
        be_made = sem("be_made")
        eps1_made, hT_begun = sem("eps1_made"), sem("hT_begun")
        pre_ready, rows_added, win_ready, added = (
            sem("pre_ready"), sem("rows_added"), sem("win_ready"), sem("added"))
        relu_done, onehot_ready = sem("relu_done"), sem("onehot_ready")
        wide_made, wide_summed, wide_added, wide_rel = (
            sem("wide_made"), sem("wide_summed"), sem("wide_added"), sem("wide_rel"))
        rows_begun = sem("rows_begun")
        part_copied, part_taken = sem("part_copied"), sem("part_taken")
        far_keyed, far_hot_ready, far_summed = sem("far_keyed"), sem("far_hot_ready"), sem("far_summed")
        far_mask_step, far_picked_step, far_row_ready = (
            sem("far_mask_step"), sem("far_picked_step"), sem("far_row_ready"))
        h1_ready, a1_ready, h2_ready = sem("h1_ready"), sem("a1_ready"), sem("h2_ready")
        y_step, squared, rooted, finished = sem("y_step"), sem("squared"), sem("rooted"), sem("finished")
        y_free = sem("y_free")

        def blocks(ap):
            return ap.rearrange("p (b f) -> p b f", f=D)


        def gather_group(pool, s, nth, tiles=TG):
            pool.wait_ge(index_loaded[s], 16 * nth)
            pool.sem_inc(rows_begun, 1)
            for t in range(tiles):
                pool.indirect_dma_start(
                    out=rows[:, s, t * D:(t + 1) * D], out_offset=None, in_=x,
                    in_offset=bass.IndirectOffsetOnAxis(ap=index[:, s, t:t + 1], axis=0),
                ).then_inc(gathered[s], 16)

        def load_group(sp, g, s):
            sp.dma_start(index[:, s, :], src[g]).then_inc(index_loaded[s], 16)
            sp.dma_start(edge[:, s, :], edges[g]).then_inc(edge_loaded[s], 16)

        def filled(turn, q):
            return 2 * turn + q // SLOTS + 1

        def is_far(q):
            return q % 2 == 1

        def gathers(turn, q, far):
            far_q = next(f for f in range(q % SLOTS, TURN, SLOTS) if is_far(f))
            if not far:
                return 16 * TG * filled(turn, q)
            left_out = (1 if q >= far_q else 0) - FAR_TURN
            return turn * (16 * (2 * TG - 1)) + 16 * (TG * (q // SLOTS + 1) - left_out)


        def pe_sums(pe, turn, q):
            s = q % SLOTS
            pe.wait_ge(rows_added, TURN * turn + q + 1)
            nc.tensor.matmul(pre[:, s, :], ones_b[:], be_group[:], start=True, stop=False)
            pe.wait_ge(edge_loaded[s], 16 * filled(turn, q))
            for h in range(HALVES):
                w = QUARTERS * D
                mm = nc.tensor.matmul(pre[:, s, h * w:(h + 1) * w], edge[:, s, h * P:(h + 1) * P], We_diag[:],
                                      start=False, stop=(h == HALVES - 1))
            mm.then_inc(pre_ready, 1)

        def dve_rows(dve, turn, q, far, last=False):
            g, s = TURN * turn + q, q % SLOTS
            dve.wait_ge(win_ready, g + 1)
            dve.wait_ge(gathered[s], gathers(turn, q, far) - (16 * (TG - TAIL_TILES) if last else 0))
            if far and is_far(q):
                dve.wait_ge(far_row_ready, far_index(turn, q) + 1)
            dve.wait_ge(pre_ready, g + 1 + SLOTS)
            nc.vector.tensor_tensor(msg[:, s, :], pre[:, s, :], rows[:, s, :], ALU.add).then_inc(rows_added, 1)

        def pe_window(pe, turn, q):
            g, s = TURN * turn + q, q % SLOTS
            pe.wait_ge(added, g + SLOTS)
            pe.wait_ge(relu_done, g + 1)
            pe.wait_ge(onehot_ready, g + 1)
            for t in range(TG):
                mm = nc.tensor.matmul(win[0:D, 0:WIN], msg[:, s, t * D:(t + 1) * D], onehot[:, s, t, :],
                                      start=(t == 0), stop=(t == TG - 1))
            mm.then_inc(win_ready, 1)

        def act_messages(act, turn, q):
            s = q % SLOTS
            act.wait_ge(rows_added, TURN * turn + q + 1 + SLOTS)
            nc.scalar.activation(msg[:, s, :], msg[:, s, :], ACT.Relu).then_inc(relu_done, 1)

        def dve_onehot(dve, turn, q):
            g, s = TURN * turn + q, q % SLOTS
            dve.wait_ge(win_ready, g + 1)
            nc.vector.tensor_tensor(
                onehot[:, s, :, :],
                win_numbers.unsqueeze(1).to_broadcast((P, TG, WIN)),
                rel[:, bass.ds(g, 1), :].rearrange("p a t -> p (a t)").unsqueeze(2).to_broadcast((P, TG, WIN)),
                ALU.is_equal).then_inc(onehot_ready, 1)

        def dve_add(dve, turn, q):
            g = TURN * turn + q
            first = dve.value_load(dst_int[0:1, bass.ds(g, 1), 0:1], min_val=0, max_val=N - 1)
            to = hT[:, bass.ds(first, WIN)]
            dve.wait_ge(win_ready, g + 1 + SLOTS)
            dve.wait_ge(added, g + SLOTS)
            nc.vector.tensor_tensor(to, win[0:D, 0:WIN], to, ALU.add).then_inc(added, 1)


        def pe_hidden(pe, c, groups_before):
            pe.wait_ge(added, groups_before + SLOTS)
            pe.wait_ge(y_step, DVE_STEPS * c + 1)
            for h, ps in enumerate((ps_half, ps_node)):
                nc.tensor.matmul(ps[:, 0:HALF], W1_wide[:], hT[:, bass.ds(c * CN + h * HALF, HALF)],
                                 start=True, stop=True).then_inc(h1_ready, 1)

        def pe_output(pe, c):
            pe.wait_ge(a1_ready, 2 * c + 2)
            for b in range(BLOCKS):
                mm = nc.tensor.matmul(ps_node[:, b * D:(b + 1) * D], a1T[:, b * P:(b + 1) * P], W2_b2[:],
                                      start=True, stop=True)
            mm.then_inc(h2_ready, 1)

        def act_load_x(act, c):
            act.wait_ge(finished, c + 1)
            act.dma_start(xc[:], x_chunks[bass.ds(c, 1)].rearrange("a p f -> (a p) f")).then_inc(x_loaded, 16)

        def act_hidden(act, c):
            for h, ps in enumerate((ps_half, ps_node)):
                act.wait_ge(h1_ready, 2 * c + 1 + h)
                nc.scalar.activation(a1T[0:D, h * HALF:(h + 1) * HALF], ps[0:D, 0:HALF], ACT.Relu,
                                     bias=b1_col[:, 0:1]).then_inc(a1_ready, 1)

        def act_norm(act, c, norm):
            centred = DVE_STEPS * c + CENTRED[norm] + 1
            act.wait_ge(y_step, centred)
            nc.scalar.activation(sq[:], y[:], ACT.Square).then_inc(squared, 1)
            act.wait_ge(y_step, centred + 1)
            nc.scalar.activation(std[:, norm, :], sq_sum[:, norm, :], ACT.Sqrt, bias=ln_eps[:, 0:1],
                                 scale=1.0 / D).then_inc(rooted, 1)

        def act_store(act, c):
            act.wait_ge(finished, c + 2)
            act.dma_start(out[bass.ds(c, 1)].rearrange("a p f -> (a p) f"), y[:]).then_inc(stored, 16)

        def act_stored(act, c):
            act.wait_ge(stored, 16 * (c + 1))
            act.sem_inc(y_free, 1)

        def dve_stepper(dve, c, steps):
            def step(ins):
                steps[0] += 1
                ins.then_inc(y_step, 1)
                dve.wait_ge(y_step, DVE_STEPS * c + 1 + steps[0])
            return step

        def per_block(ap):
            return ap.unsqueeze(2).to_broadcast((P, BLOCKS, D))

        def per_feature(ap):
            return ap.unsqueeze(1).to_broadcast((P, BLOCKS, D))

        def dve_norm(dve, c, norm, step, steps):
            step(nc.vector.tensor_reduce(row_sum[:, norm, :], blocks(y[:]), AX_X, ALU.add))
            step(nc.vector.scalar_tensor_tensor(out=blocks(y[:]), in0=per_block(row_sum[:, norm, :]), scalar=-1.0 / D,
                                                in1=blocks(y[:]), op0=ALU.mult, op1=ALU.add))
            assert steps[0] == CENTRED[norm]
            dve.wait_ge(squared, 2 * c + norm + 1)
            step(nc.vector.tensor_reduce(sq_sum[:, norm, :], blocks(sq[:]), AX_X, ALU.add))
            dve.wait_ge(rooted, 2 * c + norm + 1)
            step(nc.vector.reciprocal(rstd[:, norm, :], std[:, norm, :]))
            return nc.vector.tensor_tensor(blocks(y[:]), blocks(y[:]), per_block(rstd[:, norm, :]), ALU.mult)

        def dve_inner(dve, c):
            steps = [0]
            step = dve_stepper(dve, c, steps)
            dve.wait_ge(y_free, c + 1)
            dve.wait_ge(h2_ready, c + 1)
            step(nc.vector.tensor_scalar(y[:], ps_node[:, 0:CW], NEG_SLOPE, None, ALU.mult))
            step(nc.vector.tensor_tensor(y[:], ps_node[:, 0:CW], y[:], ALU.max))
            step(dve_norm(dve, c, 0, step, steps))
            assert steps[0] == INNER_STEPS

        def dve_outer(dve, c):
            steps = [INNER_STEPS]
            step = dve_stepper(dve, c, steps)
            step(nc.vector.tensor_tensor(blocks(y[:]), blocks(y[:]), per_feature(gamma_sb[:]), ALU.mult))
            step(nc.vector.tensor_tensor(blocks(y[:]), blocks(y[:]), per_feature(beta_sb[:]), ALU.add))
            dve.wait_ge(x_loaded, 16 * (c + 1))
            step(nc.vector.tensor_tensor(y[:], y[:], xc[:], ALU.add))
            dve_norm(dve, c, 1, step, steps).then_inc(finished, 1)
            assert steps[0] == DVE_STEPS


        def far_index(turn, q):
            return (turn - FAR_TURN) * SLOTS + q // 2

        def act_load_piece(act, r):
            act.wait_ge(part_copied, 3 * r + 1)
            act.dma_start(x_rest[:], x_classes[bass.ds(r, 1)].rearrange("a p f -> (a p) f")).then_inc(piece_loaded, 16)

        def act_copy_parts(act, r):
            act.wait_ge(piece_loaded, 16 * (r + 1))
            for part in range(3):
                if part:
                    act.wait_ge(part_taken, 2 * r + part + 1)
                nc.scalar.activation(x_parts[:, part, bass.ds(r * PIECE, PIECE)], x_rest[:], ACT.Copy).then_inc(part_copied, 1)

        def dve_take_parts(dve, r):
            for part in range(2):
                dve.wait_ge(part_copied, 3 * r + part + 2)
                nc.vector.tensor_tensor(x_rest[:], x_rest[:], x_parts[:, part, bass.ds(r * PIECE, PIECE)],
                                        ALU.subtract).then_inc(part_taken, 1)

        def dve_far_masks(dve):
            dve.wait_ge(far_col_loaded, 16)
            nc.vector.tensor_scalar(far_block[:], far_col[:], P.bit_length() - 1, CB - 1, ALU.logical_shift_right,
                                    ALU.bitwise_and).then_inc(far_mask_step, 1)
            dve.wait_ge(far_mask_step, 1)
            nc.vector.tensor_tensor(far_mask[:], far_block[:].unsqueeze(2).to_broadcast((P, NFAR, CB)),
                                    win_numbers[:, 0:CB].unsqueeze(1).to_broadcast((P, NFAR, CB)),
                                    ALU.is_equal).then_inc(far_mask_step, 1)
            dve.wait_ge(far_mask_step, 2)

        def dve_far_hot(dve, turn, q):
            i = far_index(turn, q)
            dve.wait_ge(far_loaded, 16 * (i + 1))
            nc.vector.tensor_scalar(far_key[:], far_src[:], ~((CB - 1) * P), None, ALU.bitwise_and).then_inc(far_keyed, 1)
            dve.wait_ge(far_keyed, i + 2)
            dve.wait_ge(far_summed, i + 1)
            nc.vector.tensor_tensor(far_hot[:], far_key[:].unsqueeze(1).to_broadcast((P, NCLASSES, P)),
                                    class_nodes.unsqueeze(2).to_broadcast((P, NCLASSES, P)),
                                    ALU.is_equal).then_inc(far_hot_ready, 1)

        def pe_far(pe, turn, q):
            i = far_index(turn, q)
            pe.wait_ge(far_hot_ready, i + 2)
            pe.wait_ge(far_picked_step, 2 * i + 1)
            for k in range(NCLASSES):
                for part in range(3):
                    mm = nc.tensor.matmul(far_x[:], far_hot[:, k, :], x_parts[:, part, k * CX:(k + 1) * CX],
                                          start=(k == 0 and part == 0), stop=(k == NCLASSES - 1 and part == 2))
            mm.then_inc(far_summed, 1)

        def dve_far_pick(dve, turn, q):
            i = far_index(turn, q)
            dve.wait_ge(far_summed, i + 2)
            dve.wait_ge(far_picked_step, 2 * i + 1)
            nc.vector.tensor_tensor(
                far_picked[:], far_x[:].rearrange("p (f b) -> p f b", b=CB),
                far_mask[:, bass.ds(i, 1), :].to_broadcast((P, D, CB)), ALU.mult).then_inc(far_picked_step, 1)
            dve.wait_ge(far_picked_step, 2 * i + 2)
            dve.wait_ge(rows_added, TURN * turn + q + 1)
            reduced = nc.vector.tensor_reduce(rows[:, q % SLOTS, (TG - 1) * D:], far_picked[:], AX_X, ALU.add)
            reduced.then_inc(far_row_ready, 1)
            dve.wait_ge(far_row_ready, i + 1)
            dve.sem_inc(far_picked_step, 1)


        def sp_group(sp, turn, q, far):
            g, s = TURN * turn + q, q % SLOTS
            before = gathers(turn, q - SLOTS, far) if q >= SLOTS else gathers(turn - 1, q + SLOTS, far)
            sp.wait_ge(gathered[s], before)
            sp.dma_start(index[:, s, :], src[bass.ds(g, 1)].rearrange("a p t -> (a p) t")).then_inc(index_loaded[s], 16)
            sp.wait_ge(pre_ready, g + 1)
            sp.dma_start(edge[:, s, :], edges[bass.ds(g, 1)].rearrange("a p e -> (a p) e")).then_inc(edge_loaded[s], 16)

        def sp_far(sp, turn, q):
            i = far_index(turn, q)
            sp.wait_ge(far_hot_ready, i + 1)
            sp.dma_start(far_src[:], far_rows[bass.ds(i, 1), :].to_broadcast((P, P))).then_inc(far_loaded, 16)

        def pool_group(pool, turn, q, far):
            pool.wait_ge(rows_added, TURN * turn + q + 1)
            gather_group(pool, q % SLOTS, filled(turn, q), TG - 1 if far and is_far(q) else TG)

        def pool_tail(pool):
            pool.wait_ge(rows_added, NG)
            gather_group(pool, 0, filled(TURNS, 0), TAIL_TILES)

        def windowed(eng):
            eng.wait_ge(flag_made, 1)
            return eng.value_load(flag[0:1, 0:1], min_val=0, max_val=1) == 1

        with nc.Block() as block:
            @block.sync
            def _(sp):
                for s in range(SLOTS):
                    sp.dma_start(index[:, s, :], src[s]).then_inc(index_loaded[s], 16)
                with nc.allow_non_contiguous_dma(reason="one dst of each group"):
                    sp.dma_start(first_int[:], dst[0:1, :, 0]).then_inc(first_loaded, 16)
                sp.wait_ge(diag_zero, 1)
                for q in range(QUARTERS):
                    sp.dma_start(We_diag[q * ED:(q + 1) * ED, q * D:(q + 1) * D], We).then_inc(diag_loaded, 16)
                sp.dma_start(W1_wide[:, 0:D], W1).then_inc(diag_loaded, 16)
                sp.dma_start(const[:], consts).then_inc(const_loaded, 16)
                sp.dma_start(dst_int[:], dst).then_inc(dst_loaded, 16)
                for s in range(SLOTS):
                    sp.dma_start(edge[:, s, :], edges[s]).then_inc(edge_loaded[s], 16)
                sp.dma_start(far_col[:], far_cols).then_inc(far_col_loaded, 16)

                sp_far(sp, FAR_TURN, 1)
                for q in range(SLOTS, TURN):
                    sp_group(sp, 0, q, far=False)
                with sp.If(windowed(sp)):
                    with sp.Fori(1, FAR_TURN) as turn:
                        for q in range(TURN):
                            sp_group(sp, turn, q, far=False)
                    def far_turn(turn, more_far):
                        for q in range(TURN):
                            sp_group(sp, turn, q, far=True)
                            if is_far(q + 3) and (more_far or q + 3 < TURN):
                                sp_far(sp, turn, q + 3)

                    with sp.Fori(FAR_TURN, TURNS - 1) as turn:
                        far_turn(turn, more_far=True)
                    far_turn(TURNS - 1, more_far=False)
                    sp_group(sp, TURNS, 0, far=True)
                with sp.Else():
                    with sp.Fori(1, TURNS) as turn:
                        for q in range(TURN):
                            sp_group(sp, turn, q, far=False)
                    sp_group(sp, TURNS, 0, far=False)

            @block.gpsimd
            def _(pool):
                for s in range(SLOTS):
                    gather_group(pool, s, 1)

                for q in range(SLOTS, TURN):
                    pool_group(pool, 0, q, far=False)
                with pool.If(windowed(pool)):
                    with pool.Fori(1, FAR_TURN) as turn:
                        for q in range(TURN):
                            pool_group(pool, turn, q, far=False)
                    with pool.Fori(FAR_TURN, TURNS) as turn:
                        for q in range(TURN):
                            pool_group(pool, turn, q, far=True)
                    pool_tail(pool)
                with pool.Else():
                    with pool.Fori(1, TURNS) as turn:
                        for q in range(TURN):
                            pool_group(pool, turn, q, far=False)
                    pool_tail(pool)

            @block.scalar
            def _(act):
                params = [(eps_col[:], eps.to_broadcast((D, 1))),
                          (be_all[:], be.to_broadcast((P, D))),
                          (W2_b2[0:D, :], W2), (W2_b2[D:D + 1, :], b2), (b1_col[:], b1),
                          (gamma_sb[:], gamma.to_broadcast((P, D))),
                          (beta_sb[:], beta.to_broadcast((P, D)))]
                assert len(params) == PARAMS
                for to, of in params:
                    act.dma_start(to, of).then_inc(params_loaded, 16)
                act.wait_ge(dst_loaded, 16)
                for h in range(2):
                    act.dma_start(hT[:, h * NPAD // 2:(h + 1) * NPAD // 2],
                                  xT[:, h * NPAD // 2:(h + 1) * NPAD // 2]).then_inc(hT_loaded[h], 16)
                act.wait_ge(eps1_made, 1)
                act.wait_ge(hT_loaded[0], 16)
                nc.scalar.activation(hT[:, 0:NPAD // 2], hT[:, 0:NPAD // 2], ACT.Copy, scale=eps1[:, 0:1]).then_inc(hT_begun, 1)

                def turns(start, end):
                    with act.Fori(start, end) as turn:
                        for q in range(TURN):
                            act_messages(act, turn, q)

                def finishing_turn(c, turn):
                    act_hidden(act, c)
                    for q in range(TURN):
                        if q == 2:
                            act_norm(act, c, 0)
                        act_messages(act, turn, q)
                    act_norm(act, c, 1)
                    act_store(act, c)

                with act.If(windowed(act)):
                    act_load_x(act, 0)
                    with act.Fori(0, PIECES // 2) as turn:
                        for half in range(2):
                            act_load_piece(act, 2 * turn + half)
                            for q in range(half * SLOTS, (half + 1) * SLOTS):
                                act_messages(act, turn, q)
                            act_copy_parts(act, 2 * turn + half)
                    turns(PIECES // 2, TURNS_PER_CHUNK)
                    with act.Fori(0, NCHUNKS - 2) as c:
                        finishing_turn(c, (c + 1) * TURNS_PER_CHUNK)
                        with act.Fori(1, TURNS_PER_CHUNK) as t:
                            for q in range(TURN):
                                act_messages(act, (c + 1) * TURNS_PER_CHUNK + t, q)
                        act_stored(act, c)
                        act_load_x(act, c + 1)
                    finishing_turn(NCHUNKS - 2, TURNS - LEFT_TURNS)
                    turns(TURNS - LEFT_TURNS + 1, TURNS)
                    act_stored(act, NCHUNKS - 2)
                    act_load_x(act, NCHUNKS - 1)
                    act_messages(act, TURNS, 0)
                    act_hidden(act, NCHUNKS - 1)
                    act_norm(act, NCHUNKS - 1, 0)
                    act_norm(act, NCHUNKS - 1, 1)
                    act_store(act, NCHUNKS - 1)
                    act.wait_ge(stored, 16 * NCHUNKS)
                with act.Else():
                    turns(0, TURNS)
                    act_messages(act, TURNS, 0)
                    with act.Fori(0, NCHUNKS) as c:
                        act_load_x(act, c)
                        act_hidden(act, c)
                        act_norm(act, c, 0)
                        act_norm(act, c, 1)
                        act_store(act, c)
                        act_stored(act, c)
                    act.wait_ge(stored, 16 * NCHUNKS)

            @block.tensor
            def _(pe):
                pe.wait_ge(const_made, 1)
                pe.wait_ge(first_made, 1)
                nc.tensor.matmul(ps_node[:, 0:NG], ones[0:1, :], first_dst[:], start=True, stop=True).then_inc(base_spread, 1)
                pe.wait_ge(be_made, 1)
                pe.wait_ge(diag_loaded, 16 * (QUARTERS + 1))
                for q in range(SLOTS):
                    pe_sums(pe, 0, q)
                pe.wait_ge(counted, 1)
                nc.tensor.matmul(ps_half[0:1, 0:2], ones[:, 0:1], counts[:], start=True, stop=True).then_inc(totalled, 1)

                def last_turn(turn):
                    return isinstance(turn, int) and turn == TURNS - 1

                def group(turn, q):
                    pe_window(pe, turn, q)
                    if not (last_turn(turn) and q + SLOTS > TURN):
                        pe_sums(pe, turn, q + SLOTS)

                def pair(turn, q, output_of=None):
                    if output_of is not None:
                        pe_output(pe, output_of)
                    if not (last_turn(turn) and q + 3 >= TURN):
                        pe_far(pe, turn, q + 3)
                    group(turn, q)
                    group(turn, q + 1)

                def finishing_turn(c, turn):
                    pe_hidden(pe, c, turn * TURN)
                    pair(turn, 0, output_of=c)
                    pair(turn, 2)
                    pair(turn, 4)

                def wide_group(turn, q):
                    g, s = TURN * turn + q, q % SLOTS
                    with pe.Fori(0, NW) as w:
                        pe.wait_ge(relu_done, g + 1)
                        pe.wait_ge(wide_made, g * NW + w + 1)
                        for t in range(TG):
                            mm = nc.tensor.matmul(win[0:D, 0:GWIN], msg[:, s, t * D:(t + 1) * D],
                                                  wide_hot[:, t, :], start=(t == 0), stop=(t == TG - 1))
                        mm.then_inc(wide_summed, 1)
                    pe.wait_ge(wide_added, (g + 1) * NW)
                    pe.sem_inc(win_ready, 1)
                    if not (last_turn(turn) and q + SLOTS > TURN) and turn is not TURNS:
                        pe_sums(pe, turn, q + SLOTS)

                with pe.If(windowed(pe)):
                    with pe.Fori(0, FAR_TURN - 1) as turn:
                        for q in range(TURN):
                            group(turn, q)
                    for q in range(TURN):
                        if q == SLOTS:
                            pe_far(pe, FAR_TURN, 1)
                        group(FAR_TURN - 1, q)
                    with pe.Fori(0, NCHUNKS - 2) as c:
                        finishing_turn(c, (c + 1) * TURNS_PER_CHUNK)
                        with pe.Fori(1, TURNS_PER_CHUNK) as t:
                            for q in range(0, TURN, 2):
                                pair((c + 1) * TURNS_PER_CHUNK + t, q)
                    finishing_turn(NCHUNKS - 2, TURNS - LEFT_TURNS)
                    for turn in range(TURNS - LEFT_TURNS + 1, TURNS):
                        for q in range(0, TURN, 2):
                            pair(turn, q)
                    pe_window(pe, TURNS, 0)
                    pe_hidden(pe, NCHUNKS - 1, NG)
                    pe_output(pe, NCHUNKS - 1)
                with pe.Else():
                    with pe.Fori(0, TURNS - 1) as turn:
                        for q in range(TURN):
                            wide_group(turn, q)
                    for q in range(TURN):
                        wide_group(TURNS - 1, q)
                    wide_group(TURNS, 0)
                    with pe.Fori(0, NCHUNKS) as c:
                        pe_hidden(pe, c, 0)
                        pe_output(pe, c)

            @block.vector
            def _(dve):
                steps = [0]

                def then(ins):
                    steps[0] += 1
                    ins.then_inc(setup_step, 1)
                    dve.wait_ge(setup_step, steps[0])

                nc.vector.memset(W1_wide[:], 0.0)
                nc.vector.memset(We_diag[:], 0.0).then_inc(diag_zero, 1)
                nc.vector.memset(ones[:], 1.0).then_inc(const_made, 1)
                nc.vector.memset(ones_b[:], 1.0)
                nc.vector.memset(ln_eps[:], LN_EPS)
                nc.vector.memset(hT[:, NPAD:NPAD + WIN], 0.0)
                nc.vector.memset(a1T[D:D + 1, :], 1.0)
                for begins_at_slots in (pre_ready, rows_added, win_ready, added):
                    dve.sem_inc(begins_at_slots, SLOTS)
                for begins_at_one in (y_step, finished, y_free, wide_summed, part_copied, part_taken,
                                      far_keyed, far_hot_ready, far_summed, far_picked_step):
                    dve.sem_inc(begins_at_one, 1)
                dve.wait_ge(first_loaded, 16)
                nc.vector.tensor_copy(first_dst[:], first_int[:]).then_inc(first_made, 1)
                dve.wait_ge(params_loaded, 16 * PARAMS)
                nc.vector.tensor_scalar(eps1[:], eps_col[:], 1.0, None, ALU.add).then_inc(eps1_made, 1)
                dve.wait_ge(const_loaded, 16)
                then(nc.vector.tensor_copy(be_part[:, 0, :], be_all[:]))
                then(nc.vector.tensor_tensor(be_rest[:, 0, :], be_all[:], be_part[:, 0, :], ALU.subtract))
                then(nc.vector.tensor_copy(be_part[:, 1, :], be_rest[:, 0, :]))
                then(nc.vector.tensor_tensor(be_rest[:, 1, :], be_rest[:, 0, :], be_part[:, 1, :], ALU.subtract))
                then(nc.vector.tensor_copy(be_part[:, 2, :], be_rest[:, 1, :]))
                then(nc.vector.tensor_scalar(be_rows[:, 0, :], be_part[:, 0, :], unit[:, 0:1], None, ALU.mult))
                for k in (1, 2):
                    then(nc.vector.scalar_tensor_tensor(
                        out=be_rows[:, k, :], in0=be_part[:, k, :], scalar=unit[:, k:k + 1],
                        in1=be_rows[:, k - 1, :], op0=ALU.mult, op1=ALU.add))
                nc.vector.tensor_copy(be_group[:], be_rows[:, 2, :].unsqueeze(1).to_broadcast((P, TG, D))).then_inc(be_made, 1)
                nc.vector.tensor_copy(win_numbers, numbers[:, 0:WIN])
                then(nc.vector.tensor_copy(class_nodes, class_node))
                dve.wait_ge(base_spread, 1)
                dve.wait_ge(dst_loaded, 16)
                base = ps_node[:, 0:NG]
                then(nc.vector.tensor_tensor(rel[:], dst_int[:], base.unsqueeze(2).to_broadcast((P, NG, TG)),
                                             ALU.subtract))
                then(nc.vector.tensor_scalar(marks[:], rel[:].bitcast(U32), float(WIN), 0.0, ALU.is_lt, ALU.add,
                                             accum_out=counts[:, 0:1]))
                then(nc.vector.tensor_tensor(past[:], base, limits, ALU.is_ge))
                nc.vector.tensor_reduce(counts[:, 1:2], past[:], AX_X, ALU.add).then_inc(counted, 1)
                dve.wait_ge(totalled, 1)
                then(nc.vector.tensor_scalar(total[:], ps_half[0:1, 0:1], float(E), None, ALU.is_equal))
                nc.vector.scalar_tensor_tensor(out=flag[:], in0=ps_half[0:1, 1:2], scalar=float(P * NG), in1=total[:],
                                               op0=ALU.is_equal, op1=ALU.mult).then_inc(flag_made, 1)
                for q in range(SLOTS):
                    dve_rows(dve, 0, q, far=False)
                dve.wait_ge(hT_loaded[1], 16)
                nc.vector.tensor_scalar(hT[:, NPAD // 2:NPAD], hT[:, NPAD // 2:NPAD], eps1[:, 0:1], None,
                                        ALU.mult).then_inc(hT_begun, 1)
                dve.wait_ge(hT_begun, 2)

                def in_setup(turn, q):
                    return isinstance(turn, int) and turn == 0 and q < SLOTS

                def group(turn, q, far=False, last=False):
                    dve_onehot(dve, turn, q)
                    if not in_setup(turn, q):
                        dve_rows(dve, turn, q, far, last)
                    dve_add(dve, turn, q)

                def parting_turn(turn):
                    for half in range(2):
                        for q in range(half * SLOTS, (half + 1) * SLOTS):
                            group(turn, q)
                        dve_take_parts(dve, 2 * turn + half)

                def pair(turn, q, more_far=2):
                    for k in (q, q + 1):
                        dve_onehot(dve, turn, k)
                        dve_rows(dve, turn, k, far=True)
                    if more_far >= 1:
                        dve_far_pick(dve, turn, q + 3)
                    dve_add(dve, turn, q)
                    dve_add(dve, turn, q + 1)
                    if more_far >= 2:
                        dve_far_hot(dve, turn, q + 5)

                def finishing_turn(c, turn):
                    pair(turn, 0)
                    dve_inner(dve, c)
                    pair(turn, 2)
                    pair(turn, 4)
                    dve_outer(dve, c)

                def wide_group(turn, q, last=False):
                    g = TURN * turn + q
                    if not in_setup(turn, q):
                        dve_rows(dve, turn, q, False, last)
                    nc.vector.tensor_copy(rel_g[:], dst_int[:, bass.ds(g, 1), :].rearrange("p a t -> p (a t)")).then_inc(wide_rel, 1)
                    with dve.Fori(0, NW) as w:
                        dve.wait_ge(wide_rel, g * (NW + 1) + w + 1)
                        dve.wait_ge(wide_summed, g * NW + w + 1)
                        nc.vector.tensor_tensor(
                            wide_hot[:], numbers.unsqueeze(1).to_broadcast((P, TG, GWIN)),
                            rel_g[:].unsqueeze(2).to_broadcast((P, TG, GWIN)), ALU.is_equal).then_inc(wide_made, 1)
                        dve.wait_ge(wide_made, g * NW + w + 1)
                        nc.vector.tensor_scalar(rel_g[:], rel_g[:], -float(GWIN), None, ALU.add).then_inc(wide_rel, 1)
                        dve.wait_ge(wide_summed, g * NW + w + 2)
                        to = hT[:, bass.ds(w * GWIN, GWIN)]
                        nc.vector.tensor_tensor(to, win[0:D, 0:GWIN], to, ALU.add).then_inc(wide_added, 1)
                    dve.wait_ge(wide_rel, (g + 1) * (NW + 1))

                with dve.If(windowed(dve)):
                    parting_turn(0)
                    with dve.Fori(1, PIECES // 2) as turn:
                        parting_turn(turn)
                    dve_far_masks(dve)
                    dve_far_hot(dve, FAR_TURN, 1)
                    for q in range(TURN):
                        group(FAR_TURN - 1, q)
                        if q == SLOTS + 1:
                            dve_far_pick(dve, FAR_TURN, 1)
                            dve_far_hot(dve, FAR_TURN, 3)
                    with dve.Fori(0, NCHUNKS - 2) as c:
                        finishing_turn(c, (c + 1) * TURNS_PER_CHUNK)
                        with dve.Fori(1, TURNS_PER_CHUNK) as t:
                            for q in range(0, TURN, 2):
                                pair((c + 1) * TURNS_PER_CHUNK + t, q)
                    finishing_turn(NCHUNKS - 2, TURNS - LEFT_TURNS)
                    for turn in range(TURNS - LEFT_TURNS + 1, TURNS):
                        for q in range(0, TURN, 2):
                            pair(turn, q, more_far=(NG - 3 - (TURN * turn + q)) // 2)
                    group(TURNS, 0, far=True, last=True)
                    dve_inner(dve, NCHUNKS - 1)
                    dve_outer(dve, NCHUNKS - 1)
                with dve.Else():
                    for q in range(TURN):
                        wide_group(0, q)
                    with dve.Fori(1, TURNS) as turn:
                        for q in range(TURN):
                            wide_group(turn, q)
                    wide_group(TURNS, 0, last=True)
                    dve.wait_ge(wide_added, NG * NW)
                    with dve.Fori(0, NCHUNKS) as c:
                        dve_inner(dve, c)
                        dve_outer(dve, c)


def kernel(x, src, dst, edge_attr_32, L0_gnn_We, L0_gnn_be, L0_gnn_W1, L0_gnn_b1, L0_gnn_W2, L0_gnn_b2,
           L0_gnn_eps_gin, L0_gnn_gamma, L0_gnn_beta):
    import concourse.bacc as bacc
    from concourse.bass_utils import run_bass_kernel_spmd

    x, src, dst, edge_attr = (np.asarray(a) for a in (x, src, dst, edge_attr_32))
    epad = NG * GE - E
    x_padded = np.pad(x, ((0, NPAD - N), (0, 0)))
    src_l = np.pad(src, (0, epad)).reshape(NG, TG, P).transpose(0, 2, 1)
    dst_l = np.pad(dst, (0, epad), constant_values=-1).reshape(NG, TG, P).transpose(2, 0, 1)
    edges = np.pad(edge_attr, ((0, epad), (0, 0))).reshape(NG, HALVES, QUARTERS, P, ED)
    edges = edges.transpose(0, 2, 4, 1, 3).reshape(NG, P, HALVES * P)
    x_classes = np.pad(x, ((0, NCLASSES * CLASS - N), (0, 0))).reshape(NCLASSES, CB, P, D)
    x_classes = x_classes.transpose(2, 0, 3, 1).reshape(P, PIECES, PIECE).transpose(1, 0, 2)
    far = src_l[FAR_TURN * TURN + 1:NG - 1:2, :, TG - 1]
    chunk = np.minimum(np.arange(NG) // GROUPS_PER_CHUNK, NCHUNKS - 1)
    consts = np.concatenate([np.eye(P, 3), np.tile(np.arange(GWIN), (P, 1)), np.tile(CN * chunk, (P, 1)),
                             CLASS * np.arange(NCLASSES)[None, :] + np.arange(P)[:, None]], 1)
    given = {
        "x_rows": x,
        "x_T": x_padded.T,
        "x_chunks": x_padded.reshape(NCHUNKS, BLOCKS, P, D).transpose(0, 2, 1, 3).reshape(NCHUNKS, P, CW),
        "x_classes": x_classes,
        "src_groups": src_l,
        "dst_groups": dst_l,
        "far_rows": far,
        "far_cols": far.T,
        "edge_groups": edges,
        "consts": consts.astype(np.float32),
        "We": L0_gnn_We, "be": np.reshape(L0_gnn_be, (1, D)),
        "W1": L0_gnn_W1, "b1": np.reshape(L0_gnn_b1, (D, 1)),
        "W2": L0_gnn_W2, "b2": np.reshape(L0_gnn_b2, (1, D)),
        "eps": np.reshape(L0_gnn_eps_gin, (1, 1)),
        "gamma": np.reshape(L0_gnn_gamma, (1, D)), "beta": np.reshape(L0_gnn_beta, (1, D)),
    }
    nc = bacc.Bacc("TRN2", target_bir_lowering=False, num_devices=1)
    arrays = {name: np.ascontiguousarray(a) for name, a in given.items()}
    args = [nc.dram_tensor(name, a.shape, mybir.dt.from_np(a.dtype), kind="ExternalInput").ap()
            for name, a in arrays.items()]
    out = nc.dram_tensor("out", (NCHUNKS, P, CW), F32, kind="ExternalOutput").ap()
    build(nc, *args, out)
    got = run_bass_kernel_spmd(nc, [arrays], core_ids=[0]).results[0]["out"]
    return got.reshape(NCHUNKS, P, BLOCKS, D).transpose(0, 2, 1, 3).reshape(NPAD, D)[:N]
```
